# Optimizing a Trainium2 kernel written in Bass

```python
import numpy as np
import jax
import jax.numpy as jnp

def _softmax(x, axis=-1):
    return jax.nn.softmax(x, axis=axis)

def _gelu(x):
    return jax.nn.gelu(x, approximate=True)

def _silu(x):
    return jax.nn.silu(x)

def _sigmoid(x):
    return jax.nn.sigmoid(x)

def _layernorm(x, axis=-1, eps=1e-05):
    m = jnp.mean(x, axis=axis, keepdims=True)
    v = jnp.var(x, axis=axis, keepdims=True)
    return (x - m) / jnp.sqrt(v + eps)

def _scatter_add(tgt, idx, src, axis=0):
    return tgt.at[idx].add(src)

def _segment_sum(src, seg, n):
    return jax.ops.segment_sum(src, seg, n)
kernel_name = 'mk_adj_resnorm_d1_adj_r2_ca9b15'

def setup_inputs(seed: int=0):
    np.random.seed(seed)
    _w = jnp.asarray

    def _rec_inputs():
        import jax
        import jax.numpy as jnp
        _gk = jax.random.key(seed)
        x = -8.776e-05 + 1 * jax.random.normal(jax.random.fold_in(_gk, 1), (10000, 128), jnp.float32)
        _w = (1.0 + jnp.arange(10000, dtype=jnp.float32)) ** (-0.5)
        _w = _w / _w.mean()
        _pij = jnp.clip(0.0002 * _w[:, None] * _w[None, :], 0.0, 1.0)
        _a = jax.random.uniform(jax.random.fold_in(_gk, 2), (10000, 10000)) < _pij
        _a = jnp.logical_or(_a, jnp.eye(10000, dtype=bool))
        _af = _a.astype(jnp.float32)
        _af = _af * jax.random.uniform(jax.random.fold_in(_gk, 3), (10000, 10000), jnp.float32, 0.05, 1)
        adj = _af
        return (x, adj)
    x, adj = _rec_inputs()

    def _L0_gnn_setup():
        import jax, jax.numpy as jnp
        import numpy as np
        N_USER = 10000
        N_ITEM = 10000
        HID = 128
        key = jax.random.key(seed)
        k1, k2, k3, k4, k5, k6, k7 = jax.random.split(key, 7)
        scale = 1.0 / np.sqrt(HID)
        return {'user_feat': jax.random.normal(k1, (N_USER, HID), dtype=jnp.float32), 'item_feat': jax.random.normal(k2, (N_ITEM, HID), dtype=jnp.float32), 'adj': jax.random.uniform(k3, (N_USER, N_ITEM), dtype=jnp.float32), 'W_item': jax.random.uniform(k4, (HID, HID), dtype=jnp.float32, minval=-scale, maxval=scale), 'b_item': jax.random.uniform(k5, (HID,), dtype=jnp.float32, minval=-scale, maxval=scale), 'W_user': jax.random.uniform(k6, (HID, HID), dtype=jnp.float32, minval=-scale, maxval=scale), 'b_user': jax.random.uniform(k7, (HID,), dtype=jnp.float32, minval=-scale, maxval=scale)}
    _L0_gnn_all = _L0_gnn_setup()
    _L0_gnn_in = {k: v for k, v in _L0_gnn_all.items() if k in ('item_feat', 'W_item', 'b_item', 'W_user', 'b_user')}
    del _L0_gnn_all
    return {'x': x, 'adj': adj, 'L0_gnn_item_feat': _L0_gnn_in['item_feat'], 'L0_gnn_W_item': _L0_gnn_in['W_item'], 'L0_gnn_b_item': _L0_gnn_in['b_item'], 'L0_gnn_W_user': _L0_gnn_in['W_user'], 'L0_gnn_b_user': _L0_gnn_in['b_user']}

def reference(x, adj, L0_gnn_item_feat, L0_gnn_W_item, L0_gnn_b_item, L0_gnn_W_user, L0_gnn_b_user):
    import jax
    import jax.numpy as jnp

    def _L0_gnn_ref(user_feat, item_feat, adj, W_item, b_item, W_user, b_user):
        import jax, jax.numpy as jnp
        import numpy as np
        N_USER = 10000
        N_ITEM = 10000
        HID = 128
        h = item_feat @ W_item.T + b_item
        b = user_feat @ W_user.T + b_user
        return jax.nn.relu(adj @ h + b)
    x = _layernorm(x + _L0_gnn_ref(x, L0_gnn_item_feat, adj, L0_gnn_W_item, L0_gnn_b_item, L0_gnn_W_user, L0_gnn_b_user), axis=-1)
    return x

_drawn_inputs = setup_inputs


def setup_inputs(seed=0):
    import zlib

    import numpy as np

    out = dict(_drawn_inputs(seed))
    spreads = {}
    factors = {}
    for name, (base, spread) in spreads.items():
        noise = np.random.default_rng([zlib.crc32(name.encode()), seed]).standard_normal(out[name].shape)
        drawn = base * np.exp(spread * noise) if base else spread * noise
        out[name] = jnp.asarray(drawn.astype(out[name].dtype))
    for name, factor in factors.items():
        out[name] = (out[name] * factor).astype(out[name].dtype)
    return out
```

```python
import concourse.bass as bass
from concourse import mybir
from contextlib import ExitStack

FP32 = mybir.dt.float32
ACT = mybir.ActivationFunctionType
ALU = mybir.AluOpType

P = 128
Q = 32
NQ = P // Q
ROWS = 512
EPS = 1e-5


def column_plan(n):
    per = 26
    stride = per * Q
    sections = n // (NQ * stride)
    last = n - (NQ - 1) * stride - (per + 1) * Q
    plan = [(s * NQ * stride, per) for s in range(sections - 1)] + [(last, per + 1)]
    return stride, plan, (sections - 1) * NQ * stride - last


def gnn_layer(nc, x, adj, item_feat, w_item, b_item, w_user, b_user, out):
    N = adj.shape[0]
    stride, plan, seam = column_plan(N)
    PIECES = []
    first_block = 0
    for base, blocks in plan:
        half = blocks // 2
        PIECES.append((base, 0, half, first_block))
        PIECES.append((base, half, blocks - half, first_block + half))
        first_block += blocks
    NBLK = first_block
    NPC = len(PIECES)
    WIDE = max(nb for _, _, nb, _ in PIECES) * Q
    RAWS, TS = 3, 2
    PARTS = 3

    def parts(nb):
        cut = [nb * s // PARTS for s in range(PARTS + 1)]
        return list(zip(cut[:-1], cut[1:]))

    FULL = N // ROWS
    TAIL = -(-(N - FULL * ROWS) // Q) * Q
    NB = FULL + 1
    PAIRS = NB // 2
    assert NB % 2 == 0 and NPC % RAWS == 0 and NPC % TS == 0

    def tiles(rows):
        return [(t, min(P, rows - t * P)) for t in range(-(-rows // P))]

    ctx = ExitStack()
    with ctx:
        def sb(name, shape):
            return ctx.enter_context(nc.sbuf_tensor(name, shape, FP32))

        def pb(name):
            return ctx.enter_context(nc.psum_tensor(name, [P, ROWS], FP32))

        def sem(name):
            return ctx.enter_context(nc.semaphore(name))

        raw = [sb(f"raw{s}", [P, ROWS // Q, WIDE]) for s in range(RAWS)]
        adjT = [sb(f"adjT{s}", [P, ROWS // Q, WIDE]) for s in range(TS)]
        h = sb("h", [P, NBLK, P])
        ident = sb("ident", [P, P])
        w_nat = sb("w_nat", [P, 2, P])
        wT = sb("wT", [P, 2, P])
        b_item_all = sb("b_item_all", [P, P])
        b_user_col = sb("b_user_col", [P, 1])
        featT = [sb(f"featT{s}", [P, 4, P]) for s in range(2)]
        x_nat = [sb(f"x_nat{s}", [P, 4, P]) for s in range(2)]
        xT = [sb(f"xT{s}", [P, ROWS]) for s in range(2)]
        actT = [sb(f"actT{s}", [P, ROWS]) for s in range(2)]
        y = sb("y", [P, 4, P])
        stats = sb("stats", [P, 4, 6])
        mv = sb("mv", [P, 4, 2])
        std = sb("std", [P, 4])
        rstd = sb("rstd", [P, 4])
        normed = [sb(f"normed{s}", [P, 4, P]) for s in range(2)]
        eps = sb("eps", [P, 1])
        gate = sb("gate", [P, 1])

        acc = [pb(f"acc{s}") for s in range(2)]
        featT_ps = [pb(f"featT_ps{s}") for s in range(2)]
        h_ps = [pb(f"h_ps{s}") for s in range(2)]
        xT_ps = pb("xT_ps")
        y_ps = pb("y_ps")

        feat_at, n0 = [], 0
        for s, (base, blocks) in enumerate(plan):
            slot, off = (1, n0) if s < 2 else (2, 0)
            view = raw[slot][:, :, :].rearrange("p g w -> p (g w)")
            feat_at.append(view[:, off * P:(off + blocks) * P].rearrange("p (b f) -> p b f", f=P))
            n0 += blocks

        weights_loaded = sem("weights_loaded")
        feat_loaded = [sem(f"feat_loaded{s}") for s in range(len(plan))]
        x_loaded = [sem(f"x_loaded{s}") for s in range(2)]
        raw_loaded = [sem(f"raw_loaded{s}") for s in range(RAWS)]
        ident_step = sem("ident_step")
        wT_done = sem("wT_done")
        wT_copied = sem("wT_copied")
        featT_done = sem("featT_done")
        featT_copied = sem("featT_copied")
        h_done = sem("h_done")
        h_copied = sem("h_copied")
        h_ready = sem("h_ready")
        part_transposed = sem("part_transposed")
        piece_used = sem("piece_used")
        xT_done = sem("xT_done")
        xT_copied = sem("xT_copied")
        relu_done = sem("relu_done")
        y_transposed = sem("y_transposed")
        y_added = sem("y_added")
        stats_done = sem("stats_done")
        mv_done = sem("mv_done")
        std_done = sem("std_done")
        rstd_done = sem("rstd_done")
        normed_done = sem("normed_done")
        stored = [sem(f"stored{s}") for s in range(2)]
        eps_set = sem("eps_set")
        block = ctx.enter_context(nc.Block())

        GROUPS = [(b, min(4, NBLK - b)) for b in range(0, NBLK, 4)]

        def section_of(b):
            s = 0
            while b >= plan[s][1]:
                b -= plan[s][1]
                s += 1
            return s, b

        def over_blocks(eng, body):
            body(0, ROWS, 0, 0, True)
            body(ROWS, ROWS, 1, 1, False)
            with eng.Fori(1, PAIRS - 1) as i:
                body(i * (2 * ROWS), ROWS, i * 2, 0, False)
                body(i * (2 * ROWS) + ROWS, ROWS, i * 2 + 1, 1, False)
            body((NB - 2) * ROWS, ROWS, NB - 2, 0, False)
            body(N - TAIL, TAIL, NB - 1, 1, False)

        def x_total(n, rows, par):
            full = 16 * len(tiles(ROWS))
            if isinstance(n, int):
                return (n // 2) * full + 16 * len(tiles(rows))
            return (n - par) * (full // 2) + full

        @block.sync
        def _(sp):
            sp.dma_start(w_nat[:, 0, :], w_item).then_inc(weights_loaded, 16)
            sp.dma_start(w_nat[:, 1, :], w_user).then_inc(weights_loaded, 16)
            sp.dma_start(b_item_all[:, :], b_item.rearrange("(a n) -> a n", a=1).to_broadcast([P, P])
                         ).then_inc(weights_loaded, 16)
            sp.dma_start(b_user_col[:, :], b_user.rearrange("(n a) -> n a", a=1)).then_inc(weights_loaded, 16)
            for s, (base, blocks) in enumerate(plan):
                for q in range(NQ):
                    rows = item_feat[base + stride * q:base + stride * q + Q * blocks, :]
                    sp.dma_start(feat_at[s][Q * q:Q * (q + 1), :, :],
                                 rows.rearrange("(b j) f -> j b f", j=Q)).then_inc(feat_loaded[s], 16)

            def load_block(row, rows, n, par, first):
                if not (first or par == 1 and isinstance(n, int) and n == 1):
                    sp.wait_ge(y_added, n - 1)
                for t, m in tiles(rows):
                    sp.dma_start(x_nat[par][0:m, t, :], x[bass.ds(row + t * P, m), :]).then_inc(x_loaded[par], 16)
                for k, (base, b0, nb, _) in enumerate(PIECES):
                    slot = k % RAWS
                    if not (first and k < RAWS):
                        sp.wait_ge(part_transposed, (n * NPC + (k - RAWS + 1)) * PARTS)
                    elif k == 1:
                        sp.wait_ge(featT_done, 13)
                    elif k == 2:
                        sp.wait_ge(featT_done, len(GROUPS))
                    for q in (0, 2, 1, 3):
                        col = base + stride * q + Q * b0
                        sp.dma_start(raw[slot][Q * q:Q * (q + 1), 0:rows // Q, 0:nb * Q],
                                     adj[bass.ds(row, rows), col:col + nb * Q].rearrange("(g i) c -> i g c", i=Q)
                                     ).then_inc(raw_loaded[slot], 16)

            over_blocks(sp, load_block)

        @block.gpsimd
        def _(pool):
            nc.gpsimd.memset(ident[:, :], 0.0).then_inc(ident_step, 1)
            pool.wait_ge(ident_step, 1)
            nc.gpsimd.affine_select(out=ident[:, :], in_=ident[:, :], compare_op=ALU.not_equal, fill=1.0,
                                    base=0, pattern=[[-1, P]], channel_multiplier=1).then_inc(ident_step, 1)

        @block.tensor
        def _(pe):
            pe.wait_ge(ident_step, 2)
            pe.wait_ge(weights_loaded, 64)
            for w in range(2):
                last = nc.tensor.transpose(xT_ps[:, w * P:(w + 1) * P], w_nat[:, w, :], ident[:, :])
            last.then_inc(wT_done, 1)

            def turn_feat(g):
                b, m = GROUPS[g]
                if g >= 2:
                    pe.wait_ge(featT_copied, g - 1)
                for r in range(m):
                    s, sb_ = section_of(b + r)
                    pe.wait_ge(feat_loaded[s], 16 * NQ)
                    last = nc.tensor.transpose(featT_ps[g % 2][:, r * P:(r + 1) * P], feat_at[s][:, sb_, :], ident[:, :])
                last.then_inc(featT_done, 1)

            def make_h(g):
                b, m = GROUPS[g]
                pe.wait_ge(featT_copied, g + 1)
                if g >= 2:
                    pe.wait_ge(h_copied, g - 1)
                for r in range(m):
                    last = nc.tensor.matmul(h_ps[g % 2][:, r * P:(r + 1) * P], featT[g % 2][:, r, :], wT[:, 0, :],
                                            start=True, stop=True)
                last.then_inc(h_done, 1)

            turn_feat(0)
            pe.wait_ge(wT_copied, 1)
            for g in range(len(GROUPS)):
                if g + 1 < len(GROUPS):
                    turn_feat(g + 1)
                make_h(g)

            def turn_back(n, rows, par):
                pe.wait_ge(relu_done, n + 1)
                if not (isinstance(n, int) and n == 0):
                    pe.wait_ge(y_added, n)
                for t, m in tiles(rows):
                    last = nc.tensor.transpose(y_ps[0:m, t * P:(t + 1) * P], actT[par][:, t * P:t * P + m], ident[:, :])
                last.then_inc(y_transposed, 1)

            def product(row, rows, n, par, first):
                early = first or (isinstance(n, int) and n == 1)
                pe.wait_ge(x_loaded[par], x_total(n, rows, par))
                if first:
                    pe.wait_ge(wT_copied, 1)
                else:
                    pe.wait_ge(xT_copied, n)
                for t, m in tiles(rows):
                    last = nc.tensor.transpose(xT_ps[:, t * P:t * P + m], x_nat[par][0:m, t, :], ident[0:m, 0:m])
                last.then_inc(xT_done, 1)
                if first:
                    pe.wait_ge(h_ready, 1)
                if not early:
                    pe.wait_ge(relu_done, n - 1)
                for k, (_, _, nb, hb) in enumerate(PIECES):
                    for s, (lo, hi) in enumerate(parts(nb)):
                        pe.wait_ge(part_transposed, (n * NPC + k) * PARTS + s + 1)
                        for b in range(lo, hi):
                            last = nc.tensor.matmul(acc[par][:, 0:rows].rearrange("p (g i) -> p g i", i=Q), h[:, hb + b, :],
                                                    adjT[k % TS][:, 0:rows // Q, b * Q:(b + 1) * Q],
                                                    start=(k == 0 and b == 0), stop=(k == NPC - 1 and b == nb - 1))
                    last.then_inc(piece_used, 1)
                    if k == 0 and not first:
                        turn_back(n - 1, ROWS, 1 - par)
                    if k == 1:
                        pe.wait_ge(xT_copied, n + 1)
                        nc.tensor.matmul(acc[par][:, 0:rows], wT[:, 1, :], xT[par][:, 0:rows], start=False, stop=False)

            over_blocks(pe, product)
            turn_back(NB - 1, TAIL, 1)

        @block.scalar
        def _(act):
            act.wait_ge(wT_done, 1)
            nc.scalar.activation(wT[:, :, :].rearrange("p w h -> p (w h)"), xT_ps[:, 0:2 * P], ACT.Copy
                                 ).then_inc(wT_copied, 1)
            for g, (b, m) in enumerate(GROUPS):
                act.wait_ge(featT_done, g + 1)
                if g >= 2:
                    act.wait_ge(h_done, g - 1)
                nc.scalar.activation(featT[g % 2][:, 0:m, :].rearrange("p b f -> p (b f)"), featT_ps[g % 2][:, 0:m * P],
                                     ACT.Copy).then_inc(featT_copied, 1)

            act.wait_ge(eps_set, 1)

            def finish(n, row, rows, par, skip):
                act.wait_ge(mv_done, n + 1)
                if not (isinstance(n, int) and n == 0):
                    act.wait_ge(rstd_done, n)
                w = len(tiles(rows))
                nc.scalar.activation(std[:, 0:w], mv[:, 0:w, 1], ACT.Sqrt, bias=eps[:, 0:1]).then_inc(std_done, 1)
                act.wait_ge(normed_done, n + 1)
                for t, m in tiles(rows):
                    s = skip if t == 0 else 0
                    act.dma_start(out[bass.ds(row + t * P + s, m - s), :], normed[par][s:m, t, :]).then_inc(stored[par], 16)

            def relu(row, rows, n, par, first):
                early = first or (isinstance(n, int) and n == 1)
                act.wait_ge(xT_done, n + 1)
                if not early:
                    act.wait_ge(piece_used, (n - 1) * NPC)
                nc.scalar.activation(xT[par][:, 0:rows], xT_ps[:, 0:rows], ACT.Copy).then_inc(xT_copied, 1)
                if not first:
                    finish(n - 1, row - ROWS if rows == ROWS else (NB - 2) * ROWS, ROWS, 1 - par, 0)
                act.wait_ge(piece_used, (n + 1) * NPC)
                if not early:
                    act.wait_ge(y_transposed, n - 1)
                nc.scalar.activation(actT[par][:, 0:rows], acc[par][:, 0:rows], ACT.Relu,
                                     bias=b_user_col[:, 0:1]).then_inc(relu_done, 1)

            over_blocks(act, relu)
            finish(NB - 1, N - TAIL, TAIL, 1, FULL * ROWS - (N - TAIL))
            for par in range(2):
                act.wait_ge(stored[par], 16 * sum(len(tiles(TAIL if n == NB - 1 else ROWS)) for n in range(par, NB, 2)))

        @block.vector
        def _(dve):
            nc.vector.memset(eps[:, :], EPS).then_inc(eps_set, 1)
            dve.wait_ge(weights_loaded, 64)
            for g, (b, m) in enumerate(GROUPS):
                dve.wait_ge(h_done, g + 1)
                nc.vector.tensor_tensor(h[:, b:b + m, :], h_ps[g % 2][:, 0:m * P].rearrange("p (b f) -> p b f", f=P),
                                        b_item_all[:, :].unsqueeze(1).to_broadcast([P, m, P]), ALU.add).then_inc(h_copied, 1)
            dve.wait_ge(h_copied, len(GROUPS))
            nc.vector.memset(h[0:seam, NBLK - plan[-1][1], :], 0.0)
            nc.vector.memset(h[0:(NQ - 1) * Q, NBLK - 1, :], 0.0).then_inc(h_ready, 1)

            def turn(k, rows, n, first):
                _, _, nb, _ = PIECES[k]
                nth = n // 2 * (NPC // RAWS * 2) if isinstance(n, int) else None
                dve.wait_ge(raw_loaded[k % RAWS], raw_total(n, k))
                if not (first and k < TS):
                    dve.wait_ge(piece_used, n * NPC + (k - TS + 1))
                for lo, hi in parts(nb):
                    nc.vector.transpose(adjT[k % TS][:, 0:rows // Q, lo * Q:hi * Q],
                                        raw[k % RAWS][:, 0:rows // Q, lo * Q:hi * Q]).then_inc(part_transposed, 1)

            def raw_total(n, k):
                return (n * (NPC // RAWS) + (k // RAWS + 1)) * (16 * NQ)

            def add_and_stats(n, rows, par):
                dve.wait_ge(y_transposed, n + 1)
                w = len(tiles(rows))
                dve.wait_ge(x_loaded[par], x_total(n, rows, par))
                if not (isinstance(n, int) and n == 0):
                    dve.wait_ge(normed_done, n)
                for m, lo, hi in spans(rows):
                    last = nc.vector.tensor_tensor(y[0:m, lo:hi, :], y_ps[0:m, lo * P:hi * P].rearrange("p (t f) -> p t f", f=P),
                                                   x_nat[par][0:m, lo:hi, :], ALU.add)
                last.then_inc(y_added, 1)
                dve.wait_ge(y_added, n + 1)
                for t, m in tiles(rows):
                    last = nc.vector.bn_stats(stats[0:m, t, :], y[0:m, t, :])
                last.then_inc(stats_done, 1)
                dve.wait_ge(stats_done, n + 1)
                if not (isinstance(n, int) and n == 0):
                    dve.wait_ge(std_done, n)
                nc.vector.memset(gate[:, :], 0.0)
                for t, m in tiles(rows):
                    last = nc.vector.bn_aggr(mv[0:m, t, :], stats[0:m, t, :])
                last.then_inc(mv_done, 1)

            def spans(rows):
                full = rows // P
                return [(P, 0, full)] + ([(rows - full * P, full, full + 1)] if rows % P else [])

            def normalise(n, rows, par, early):
                w = len(tiles(rows))
                dve.wait_ge(std_done, n + 1)
                nc.vector.reciprocal(rstd[:, 0:w], std[:, 0:w]).then_inc(rstd_done, 1)
                dve.wait_ge(rstd_done, n + 1)
                if not early:
                    dve.wait_ge(stored[par], (n - par) * (8 * len(tiles(ROWS))))
                for t, m in tiles(rows):
                    last = nc.vector.tensor_scalar(normed[par][0:m, t, :], y[0:m, t, :], mv[0:m, t, 0:1], rstd[0:m, t:t + 1],
                                                   ALU.subtract, ALU.mult)
                last.then_inc(normed_done, 1)

            def transposes(row, rows, n, par, first):
                for k in range(NPC):
                    turn(k, rows, n, first)
                    if k == 2 and not first:
                        add_and_stats(n - 1, ROWS, 1 - par)
                    if k == 3 and not first:
                        normalise(n - 1, ROWS, 1 - par, isinstance(n, int) and n <= 2)

            over_blocks(dve, transposes)
            add_and_stats(NB - 1, TAIL, 1)
            normalise(NB - 1, TAIL, 1, False)


_INS = ["x", "adj", "L0_gnn_item_feat", "L0_gnn_W_item", "L0_gnn_b_item", "L0_gnn_W_user", "L0_gnn_b_user"]


def kernel(**inputs):
    import numpy as _np
    import concourse.bacc as _bacc
    from concourse import mybir as _mybir
    from concourse.bass_utils import run_bass_kernel_spmd as _run

    nc = _bacc.Bacc("TRN2", target_bir_lowering=False, num_devices=1)
    arrays, args = {}, []
    for name in _INS:
        a = _np.ascontiguousarray(inputs[name])
        arrays[f"in_{name}_dram"] = a
        args.append(nc.dram_tensor(f"in_{name}_dram", a.shape, _mybir.dt.from_np(a.dtype), kind="ExternalInput").ap())
    out = nc.dram_tensor("out_dram", inputs["x"].shape, _mybir.dt.float32, kind="ExternalOutput").ap()
    gnn_layer(nc, *args, out)
    r = _run(nc, [arrays], core_ids=[0])
    return r.results[0]["out_dram"]
```

```python
import concourse.bass as bass
from concourse import mybir
from contextlib import ExitStack

FP32 = mybir.dt.float32
FP32R = mybir.dt.float32r
ACT = mybir.ActivationFunctionType
ALU = mybir.AluOpType

P = 128
Q = 32
NQ = P // Q
ROWS = 512
G = ROWS // Q
EPS = 1e-5

SECTION = 26
PIECE = 9
PART = 3
RAWS = 3
SPLITS = 3


def column_plan(n):
    stride = SECTION * Q
    sections = n // (NQ * stride)
    last = n - (NQ - 1) * stride - (SECTION + 1) * Q
    plan = [(s * NQ * stride, SECTION) for s in range(sections - 1)] + [(last, SECTION + 1)]
    return stride, plan, (sections - 1) * NQ * stride - last


def gnn_layer(nc, x, adj, item_feat, w_item, b_item, w_user, b_user, out):
    N = adj.shape[0]
    stride, plan, seam = column_plan(N)
    PIECES = [(s, b0, min(PIECE, blocks - b0)) for s, (_, blocks) in enumerate(plan) for b0 in range(0, blocks, PIECE)]
    NPC = len(PIECES)

    def parts(k):
        nb = PIECES[k][2]
        return [(True, 0, PART), (True, nb - PART, nb), (False, PART, nb - PART)]

    NS = 2 * NPC
    LOW_AFTER = {6: 3, 15: 9, 24: 15}
    ON_DVE = [s for s in range(NS) if s in LOW_AFTER.values()]
    ON_POOL = [s for s in range(NS) if s not in ON_DVE]
    FULL = N // ROWS
    TAIL = -(-(N - FULL * ROWS) // Q) * Q
    NB = FULL + 1
    PAIRS = NB // 2
    assert PIECES[-1][2] == PIECE and all(nb < PIECE for _, _, nb in PIECES[(NPC - 1) % RAWS:-1:RAWS])
    assert NB % 2 == 0 and NPC % RAWS == 0 and NS % SPLITS == 0

    def tiles(rows):
        return [(t, min(P, rows - t * P)) for t in range(-(-rows // P))]

    ctx = ExitStack()
    with ctx:
        def sb(name, shape, dt=FP32):
            return ctx.enter_context(nc.sbuf_tensor(name, shape, dt))

        def pb(name):
            return ctx.enter_context(nc.psum_tensor(name, [P, ROWS], FP32))

        def sem(name):
            return ctx.enter_context(nc.semaphore(name))

        raw = [sb(f"raw{s}", [P, G, PIECE * Q]) for s in range(RAWS)]
        turned_s = sb("turned_s", [P, 4, G, PART * Q])
        turned_f = sb("turned_f", [P, G, PART * Q])
        high = [sb(f"high{s}", [P, G, PART * Q], FP32R) for s in range(SPLITS)]
        low = [sb(f"low{s}", [P, G, PART * Q], FP32R) for s in range(SPLITS)]
        h_high = sb("h_high", [P, NS, PART, P], FP32R)
        h_low = sb("h_low", [P, NS, PART, P], FP32R)
        h_full = sb("h_full", [P, NPC, PART, P])
        ident = sb("ident", [P, P])
        wT = sb("wT", [P, 2, P])
        b_item_all = sb("b_item_all", [P, P])
        b_user_col = sb("b_user_col", [P, 1])
        x_nat = [sb(f"x_nat{s}", [P, 4, P]) for s in range(2)]
        xT = sb("xT", [P, ROWS])
        actT = sb("actT", [P, ROWS])
        y = [sb(f"y{s}", [P, 4, P]) for s in range(2)]
        stats = sb("stats", [P, 4, 6])
        mv = sb("mv", [P, 4, 2])
        std = sb("std", [P, 4])
        rstd = sb("rstd", [P, 4])
        eps = sb("eps", [P, 1])
        gate = sb("gate", [P, 1])

        acc = [pb(f"acc{s}") for s in range(2)]
        featT_ps = [pb(f"featT_ps{s}") for s in range(2)]
        h_ps = [pb(f"h_ps{s}") for s in range(2)]
        xT_ps = pb("xT_ps")
        y_ps = pb("y_ps")

        w_nat = x_nat[1][:, 0:2, :]
        featT = [t[:, 0:PART * P].rearrange("p (b f) -> p b f", f=P) for t in (xT, actT)]
        h_stage = [t[:, 0:PART, :] for t in y]
        feat_at = [v.rearrange("p (b f) -> p b f", f=P)[:, 0:blocks, :] for (_, blocks), v in zip(
            plan, [turned_s[:, :, :, :].rearrange("p a g w -> p (a g w)")]
            + [raw[s][:, :, :].rearrange("p g w -> p (g w)") for s in (1, 2)])]

        w_loaded = sem("w_loaded")
        feat_loaded = [sem(f"feat_loaded{s}") for s in range(NPC)]
        x_loaded = [sem(f"x_loaded{s}") for s in range(2)]
        raw_loaded = [sem(f"raw_loaded{s}") for s in range(RAWS)]
        ident_step = sem("ident_step")
        wT_done = sem("wT_done")
        wT_copied = sem("wT_copied")
        featT_done = sem("featT_done")
        featT_copied = sem("featT_copied")
        h_done = sem("h_done")
        h_biased = sem("h_biased")
        h_masked = sem("h_masked")
        h_high_done = sem("h_high_done")
        h_low_done = sem("h_low_done")
        turned = sem("turned")
        high_done = sem("high_done")
        low_by_pool = sem("low_by_pool")
        low_by_dve = sem("low_by_dve")
        split_used = sem("split_used")
        full_used = sem("full_used")
        xT_done = sem("xT_done")
        xT_copied = sem("xT_copied")
        xT_used = sem("xT_used")
        relu_done = sem("relu_done")
        y_turned = sem("y_turned")
        y_added = sem("y_added")
        stats_done = sem("stats_done")
        mv_done = sem("mv_done")
        std_done = sem("std_done")
        rstd_done = sem("rstd_done")
        normed = sem("normed")
        stored = [sem(f"stored{s}") for s in range(2)]
        eps_set = sem("eps_set")
        pad_zeroed = sem("pad_zeroed")
        block = ctx.enter_context(nc.Block())

        GROUPS = [(k, j, split, PIECES[k][1] + lo, hi - lo) for k in range(NPC) for j, (split, lo, hi) in enumerate(parts(k))]
        READ = [sum(3 for s, _, _ in PIECES if s <= t) for t in range(len(plan))]
        MASKED = [g for g, (k, _, _, b, m) in enumerate(GROUPS) if PIECES[k][0] == len(plan) - 1 and (b == 0 or b + m == plan[-1][1])]
        SPLIT_GROUPS = [g for g, group in enumerate(GROUPS) if group[2]]

        def wait(eng, semaphore, count):
            if not (isinstance(count, int) and count <= 0):
                eng.wait_ge(semaphore, count)

        def over_blocks(eng, body):
            body(0, ROWS, 0, 0)
            body(ROWS, ROWS, 1, 1)
            with eng.Fori(1, PAIRS - 1) as i:
                body(i * (2 * ROWS), ROWS, i * 2, 0)
                body(i * (2 * ROWS) + ROWS, ROWS, i * 2 + 1, 1)
            body((NB - 2) * ROWS, ROWS, NB - 2, 0)
            body(N - TAIL, TAIL, NB - 1, 1)

        def is_first(n):
            return isinstance(n, int) and n == 0

        def x_total(n, rows, par):
            if isinstance(n, int):
                return (n // 2) * 16 * len(tiles(ROWS)) + 16 * len(tiles(rows))
            return (n - par) * (8 * len(tiles(ROWS))) + 16 * len(tiles(ROWS))

        def s_slot(k, par, j):
            return 2 * ((NPC * par + k) % 2) + j

        def load_feat(eng, k, quarters):
            s, b0, nb = PIECES[k]
            for q in quarters:
                row = plan[s][0] + stride * q + Q * b0
                eng.dma_start(feat_at[s][Q * q:Q * (q + 1), b0:b0 + nb, :],
                              item_feat[row:row + Q * nb, :].rearrange("(b j) f -> j b f", j=Q)).then_inc(feat_loaded[k], 16)

        def load_piece(eng, k, row, rows, quarters):
            s, b0, nb = PIECES[k]
            for q in quarters:
                col = plan[s][0] + stride * q + Q * b0
                w = nb * Q if k < NPC - 1 or q == NQ - 1 else (nb - 1) * Q
                eng.dma_start(raw[k % RAWS][Q * q:Q * (q + 1), 0:rows // Q, 0:w],
                              adj[bass.ds(row, rows), col:col + w].rearrange("(g i) c -> i g c", i=Q)
                              ).then_inc(raw_loaded[k % RAWS], 16)

        @block.sync
        def _(sp):
            sp.dma_start(w_nat[:, 0, :], w_item).then_inc(w_loaded, 16)
            sp.dma_start(w_nat[:, 1, :], w_user).then_inc(w_loaded, 16)
            sp.dma_start(b_item_all[:, :], b_item.rearrange("(a n) -> a n", a=1).to_broadcast([P, P])
                         ).then_inc(w_loaded, 16)
            sp.dma_start(b_user_col[:, :], b_user.rearrange("(n a) -> n a", a=1)).then_inc(w_loaded, 16)
            for k in range(NPC):
                load_feat(sp, k, (0, 2, 1, 3))

            def load_block(row, rows, n, par):
                if isinstance(n, int) and n == 1:
                    sp.wait_ge(wT_done, 1)
                wait(sp, y_added, n - 1)
                for t, m in tiles(rows):
                    sp.dma_start(x_nat[par][0:m, t, :], x[bass.ds(row + t * P, m), :]).then_inc(x_loaded[par], 16)
                for k in range(NPC):
                    wait(sp, turned, (n * NPC + (k - RAWS + 1)) * 3)
                    if is_first(n) and k in (1, 2):
                        sp.wait_ge(featT_done, READ[k])
                    load_piece(sp, k, row, rows, (0, 1))

            over_blocks(sp, load_block)

        @block.gpsimd
        def _(pool):
            nc.gpsimd.memset(ident[:, :], 0.0).then_inc(ident_step, 1)
            pool.wait_ge(ident_step, 1)
            nc.gpsimd.affine_select(out=ident[:, :], in_=ident[:, :], compare_op=ALU.not_equal, fill=1.0,
                                    base=0, pattern=[[-1, P]], channel_multiplier=1).then_inc(ident_step, 1)
            for i, g in enumerate(SPLIT_GROUPS):
                pool.wait_ge(h_high_done, i + 1)
                nc.gpsimd.tensor_tensor(h_low[:, i, :, :], h_stage[i % 2], h_high[:, i, :, :].bitcast(FP32),
                                        ALU.subtract).then_inc(h_low_done, 1)

            pool.wait_ge(featT_done, len(GROUPS))
            nc.gpsimd.memset(raw[(NPC - 1) % RAWS][0:(NQ - 1) * Q, :, (PIECE - 1) * Q:PIECE * Q], 0.0).then_inc(pad_zeroed, 1)

            def low_parts(row, rows, n, par):
                for i, s in enumerate(ON_POOL):
                    k, j = s // 2, s % 2
                    pool.wait_ge(high_done, n * NS + s + 1)
                    wait(pool, split_used, n * NS + s + 1 - SPLITS)
                    nc.gpsimd.tensor_tensor(low[s % SPLITS][:, 0:rows // Q, :], turned_s[:, s_slot(k, par, j), 0:rows // Q, :],
                                            high[s % SPLITS][:, 0:rows // Q, :].bitcast(FP32), ALU.subtract
                                            ).then_inc(low_by_pool, 1)

            over_blocks(pool, low_parts)

        def wait_low(eng, n, s):
            if s in ON_DVE:
                wait(eng, low_by_dve, n * len(ON_DVE) + ON_DVE.index(s) + 1)
            else:
                wait(eng, low_by_pool, n * len(ON_POOL) + ON_POOL.index(s) + 1)

        @block.tensor
        def _(pe):
            pe.wait_ge(ident_step, 2)
            pe.wait_ge(w_loaded, 64)
            for w in range(2):
                last = nc.tensor.transpose(xT_ps[:, w * P:(w + 1) * P], w_nat[:, w, :], ident[:, :])
            last.then_inc(wT_done, 1)

            def turn_feat(g):
                k, _, _, b, m = GROUPS[g]
                s = PIECES[k][0]
                wait(pe, featT_copied, g - 1)
                pe.wait_ge(feat_loaded[k], 16 * NQ)
                for r in range(m):
                    last = nc.tensor.transpose(featT_ps[g % 2][:, r * P:(r + 1) * P], feat_at[s][:, b + r, :], ident[:, :])
                last.then_inc(featT_done, 1)

            def make_h(g):
                m = GROUPS[g][4]
                pe.wait_ge(featT_copied, g + 1)
                wait(pe, h_biased, g - 1)
                for r in range(m):
                    last = nc.tensor.matmul(h_ps[g % 2][:, r * P:(r + 1) * P], featT[g % 2][:, r, :], wT[:, 0, :],
                                            start=True, stop=True)
                last.then_inc(h_done, 1)

            turn_feat(0)
            pe.wait_ge(wT_copied, 1)
            for g in range(len(GROUPS)):
                if g + 1 < len(GROUPS):
                    turn_feat(g + 1)
                make_h(g)

            def turn_x(n, rows, par):
                pe.wait_ge(x_loaded[par], x_total(n, rows, par))
                wait(pe, xT_copied, n)
                for t, m in tiles(rows):
                    last = nc.tensor.transpose(xT_ps[:, t * P:t * P + m], x_nat[par][0:m, t, :], ident[0:m, 0:m])
                last.then_inc(xT_done, 1)

            def turn_back(n, rows):
                pe.wait_ge(relu_done, n + 1)
                wait(pe, y_added, n)
                for t, m in tiles(rows):
                    last = nc.tensor.transpose(y_ps[0:m, t * P:(t + 1) * P], actT[:, t * P:t * P + m], ident[:, :])
                last.then_inc(y_turned, 1)

            def product(row, rows, n, par):
                g = rows // Q
                total = acc[par][:, 0:rows].rearrange("p (g i) -> p g i", i=Q)

                def add(weights, moving, b, first=False, final=False):
                    return nc.tensor.matmul(total, weights, moving[:, 0:g, b * Q:(b + 1) * Q], start=first, stop=final)

                wait(pe, relu_done, n - 1)
                for k in range(NPC):
                    nf = PIECES[k][2] - 2 * PART
                    pe.wait_ge(turned, (n * NPC + k + 1) * 3)
                    for b in range(nf):
                        last = add(h_full[:, k, b, :], turned_f, b, first=(k == 0 and b == 0))
                    last.then_inc(full_used, 1)
                    for s in (2 * k, 2 * k + 1):
                        hi, lo = high[s % SPLITS], low[s % SPLITS]
                        pe.wait_ge(high_done, n * NS + s + 1)
                        for b in range(PART):
                            add(h_high[:, s, b, :], hi, b)
                            add(h_low[:, s, b, :], hi, b)
                        wait_low(pe, n, s)
                        for b in range(PART):
                            last = add(h_high[:, s, b, :], lo, b, final=(s == NS - 1 and b == PART - 1))
                        last.then_inc(split_used, 1)
                    if k == 0 and not is_first(n):
                        turn_back(n - 1, ROWS)
                    if k == 1:
                        turn_x(n, rows, par)
                    if k == 3:
                        pe.wait_ge(xT_copied, n + 1)
                        nc.tensor.matmul(acc[par][:, 0:rows], wT[:, 1, :], xT[:, 0:rows], start=False, stop=False
                                         ).then_inc(xT_used, 1)

            pe.wait_ge(h_biased, len(GROUPS))
            pe.wait_ge(h_high_done, NS)
            pe.wait_ge(h_low_done, NS)
            over_blocks(pe, product)
            turn_back(NB - 1, TAIL)

        @block.scalar
        def _(act):
            load_piece(act, 0, 0, ROWS, (2, 3))
            act.wait_ge(wT_done, 1)
            nc.scalar.activation(wT[:, :, :].rearrange("p w h -> p (w h)"), xT_ps[:, 0:2 * P], ACT.Copy
                                 ).then_inc(wT_copied, 1)

            def copy_featT(g):
                m = GROUPS[g][4]
                act.wait_ge(featT_done, g + 1)
                wait(act, h_done, g - 1)
                nc.scalar.activation(featT[g % 2][:, 0:m, :].rearrange("p b f -> p (b f)"), featT_ps[g % 2][:, 0:m * P],
                                     ACT.Copy).then_inc(featT_copied, 1)

            def split_h(i):
                g = SPLIT_GROUPS[i]
                act.wait_ge(h_biased, g + 1)
                if g in MASKED:
                    act.wait_ge(h_masked, MASKED.index(g) + 1)
                nc.scalar.activation(h_high[:, i, :, :], h_stage[i % 2], ACT.Copy).then_inc(h_high_done, 1)

            for g in range(len(GROUPS)):
                copy_featT(g)
                for k in (1, 2):
                    if g == READ[k]:
                        load_piece(act, k, 0, ROWS, (2, 3))
                if g >= 2 and g - 2 in SPLIT_GROUPS:
                    split_h(SPLIT_GROUPS.index(g - 2))
            for g in SPLIT_GROUPS:
                if g + 2 >= len(GROUPS):
                    split_h(SPLIT_GROUPS.index(g))

            if READ[2] == len(GROUPS):
                load_piece(act, 2, 0, ROWS, (2, 3))
            act.wait_ge(eps_set, 1)

            def deviation(n, rows):
                act.wait_ge(mv_done, n + 1)
                wait(act, rstd_done, n)
                w = len(tiles(rows))
                nc.scalar.activation(std[:, 0:w], mv[:, 0:w, 1], ACT.Sqrt, bias=eps[:, 0:1]).then_inc(std_done, 1)

            def store(n, row, rows, par, skip):
                act.wait_ge(normed, n + 1)
                for t, m in tiles(rows):
                    s = skip if t == 0 else 0
                    act.dma_start(out[bass.ds(row + t * P + s, m - s), :], y[par][s:m, t, :]).then_inc(stored[par], 16)

            def relu(n, rows, par):
                act.wait_ge(split_used, (n + 1) * NS)
                wait(act, y_turned, n)
                nc.scalar.activation(actT[:, 0:rows], acc[par][:, 0:rows], ACT.Relu,
                                     bias=b_user_col[:, 0:1]).then_inc(relu_done, 1)

            def high_parts(row, rows, n, par):
                before = row - ROWS if rows == ROWS else (NB - 2) * ROWS
                for s in range(NS):
                    k, j = s // 2, s % 2
                    act.wait_ge(turned, (n * NPC + k) * 3 + j + 1)
                    wait(act, split_used, n * NS + s + 1 - SPLITS)
                    nc.scalar.activation(high[s % SPLITS][:, 0:rows // Q, :], turned_s[:, s_slot(k, par, j), 0:rows // Q, :],
                                         ACT.Copy).then_inc(high_done, 1)
                    if j == 1 and k < NPC - RAWS:
                        act.wait_ge(turned, (n * NPC + k + 1) * 3)
                        load_piece(act, k + RAWS, row, rows, (2, 3))
                    elif j == 1 and rows == ROWS:
                        act.wait_ge(turned, (n * NPC + k + 1) * 3)
                        nxt = (N - TAIL, TAIL) if isinstance(n, int) and n == NB - 2 else (row + ROWS, ROWS)
                        load_piece(act, k + RAWS - NPC, *nxt, (2, 3))
                    if s == 1 and not is_first(n):
                        relu(n - 1, ROWS, 1 - par)
                    if s == 2 * 2 + 1:
                        act.wait_ge(xT_done, n + 1)
                        wait(act, xT_used, n)
                        nc.scalar.activation(xT[:, 0:rows], xT_ps[:, 0:rows], ACT.Copy).then_inc(xT_copied, 1)
                    if s == 2 * 3 + 1 and not is_first(n):
                        deviation(n - 1, ROWS)
                    if s == 2 * 6 + 1 and not is_first(n):
                        store(n - 1, before, ROWS, 1 - par, 0)

            over_blocks(act, high_parts)
            relu(NB - 1, TAIL, 1)
            deviation(NB - 1, TAIL)
            store(NB - 1, N - TAIL, TAIL, 1, FULL * ROWS - (N - TAIL))
            for par in range(2):
                act.wait_ge(stored[par], 16 * sum(len(tiles(TAIL if n == NB - 1 else ROWS)) for n in range(par, NB, 2)))

        @block.vector
        def _(dve):
            nc.vector.memset(eps[:, :], EPS).then_inc(eps_set, 1)
            dve.wait_ge(w_loaded, 64)

            def bias_h(g):
                k, j, split, b, m = GROUPS[g]
                dve.wait_ge(h_done, g + 1)
                if split:
                    i = SPLIT_GROUPS.index(g)
                    wait(dve, h_low_done, i - 1)
                    dst = h_stage[i % 2]
                else:
                    dst = h_full[:, k, 0:m, :]
                last = nc.vector.tensor_tensor(dst, h_ps[g % 2][:, 0:m * P].rearrange("p (b f) -> p b f", f=P),
                                               b_item_all[:, :].unsqueeze(1).to_broadcast([P, m, P]), ALU.add)
                last.then_inc(h_biased, 1)
                if g in MASKED:
                    dve.wait_ge(h_biased, g + 1)
                    if g == MASKED[0]:
                        nc.vector.memset(h_stage[i % 2][0:seam, 0, :], 0.0).then_inc(h_masked, 1)
                    else:
                        nc.vector.memset(h_stage[i % 2][0:(NQ - 1) * Q, m - 1, :], 0.0).then_inc(h_masked, 1)

            def turn(k, rows, n, par):
                if is_first(n) and k == NPC - 1:
                    dve.wait_ge(pad_zeroed, 1)
                dve.wait_ge(raw_loaded[k % RAWS], (n * (NPC // RAWS) + (k // RAWS + 1)) * (16 * NQ))
                for j, (split, lo, hi) in enumerate(parts(k)):
                    if split:
                        s = 2 * k + j
                        if s >= 4:
                            wait_low(dve, n, s - 4)
                        elif not is_first(n):
                            wait_low(dve, n - 1, s - 4 + NS)
                        dst = turned_s[:, s_slot(k, par, j), 0:rows // Q, :]
                    else:
                        wait(dve, full_used, n * NPC + k)
                        dst = turned_f[:, 0:rows // Q, 0:(hi - lo) * Q]
                    nc.vector.transpose(dst, raw[k % RAWS][:, 0:rows // Q, lo * Q:hi * Q]).then_inc(turned, 1)
                    if 3 * k + j in LOW_AFTER:
                        low_part(LOW_AFTER[3 * k + j], rows, n, par)

            def low_part(s, rows, n, par):
                k, j = s // 2, s % 2
                dve.wait_ge(high_done, n * NS + s + 1)
                wait(dve, split_used, n * NS + s + 1 - SPLITS)
                nc.vector.tensor_tensor(low[s % SPLITS][:, 0:rows // Q, :], turned_s[:, s_slot(k, par, j), 0:rows // Q, :],
                                        high[s % SPLITS][:, 0:rows // Q, :].bitcast(FP32), ALU.subtract
                                        ).then_inc(low_by_dve, 1)

            def add_and_stats(n, rows, par):
                dve.wait_ge(y_turned, n + 1)
                dve.wait_ge(x_loaded[par], x_total(n, rows, par))
                if isinstance(n, int):
                    done = n // 2 * 16 * len(tiles(ROWS))
                else:
                    done = (n - par) * (8 * len(tiles(ROWS)))
                wait(dve, stored[par], done)
                full = rows // P
                for m, lo, hi in [(P, 0, full)] + ([(rows - full * P, full, full + 1)] if rows % P else []):
                    last = nc.vector.tensor_tensor(y[par][0:m, lo:hi, :], y_ps[0:m, lo * P:hi * P].rearrange("p (t f) -> p t f", f=P),
                                                   x_nat[par][0:m, lo:hi, :], ALU.add)
                last.then_inc(y_added, 1)
                dve.wait_ge(y_added, n + 1)
                for t, m in tiles(rows):
                    last = nc.vector.bn_stats(stats[0:m, t, :], y[par][0:m, t, :])
                last.then_inc(stats_done, 1)
                dve.wait_ge(stats_done, n + 1)
                wait(dve, std_done, n)
                nc.vector.memset(gate[:, :], 0.0)
                for t, m in tiles(rows):
                    last = nc.vector.bn_aggr(mv[0:m, t, :], stats[0:m, t, :])
                last.then_inc(mv_done, 1)

            def normalise(n, rows, par):
                w = len(tiles(rows))
                dve.wait_ge(std_done, n + 1)
                nc.vector.reciprocal(rstd[:, 0:w], std[:, 0:w]).then_inc(rstd_done, 1)
                dve.wait_ge(rstd_done, n + 1)
                for t, m in tiles(rows):
                    last = nc.vector.tensor_scalar(y[par][0:m, t, :], y[par][0:m, t, :], mv[0:m, t, 0:1], rstd[0:m, t:t + 1],
                                                   ALU.subtract, ALU.mult)
                last.then_inc(normed, 1)

            def transposes(row, rows, n, par):
                for k in range(NPC):
                    if not (is_first(n) and k == 0):
                        turn(k, rows, n, par)
                    if k == 2 and not is_first(n):
                        add_and_stats(n - 1, ROWS, 1 - par)
                    if k == 4 and not is_first(n):
                        normalise(n - 1, ROWS, 1 - par)

            for g in range(24):
                bias_h(g)
            turn(0, ROWS, 0, 0)
            for g in range(24, len(GROUPS)):
                bias_h(g)
            over_blocks(dve, transposes)
            add_and_stats(NB - 1, TAIL, 1)
            normalise(NB - 1, TAIL, 1)


_INS = ["x", "adj", "L0_gnn_item_feat", "L0_gnn_W_item", "L0_gnn_b_item", "L0_gnn_W_user", "L0_gnn_b_user"]


def kernel(**inputs):
    import numpy as _np
    import concourse.bacc as _bacc
    from concourse import mybir as _mybir
    from concourse.bass_utils import run_bass_kernel_spmd as _run

    nc = _bacc.Bacc("TRN2", target_bir_lowering=False, num_devices=1)
    arrays, args = {}, []
    for name in _INS:
        a = _np.ascontiguousarray(inputs[name])
        arrays[f"in_{name}_dram"] = a
        args.append(nc.dram_tensor(f"in_{name}_dram", a.shape, _mybir.dt.from_np(a.dtype), kind="ExternalInput").ap())
    out = nc.dram_tensor("out_dram", inputs["x"].shape, _mybir.dt.float32, kind="ExternalOutput").ap()
    gnn_layer(nc, *args, out)
    r = _run(nc, [arrays], core_ids=[0])
    return r.results[0]["out_dram"]
```

```python
import concourse.bass as bass
from concourse import mybir
from contextlib import ExitStack

FP32 = mybir.dt.float32
FP32R = mybir.dt.float32r
ACT = mybir.ActivationFunctionType
ALU = mybir.AluOpType

P = 128
Q = 32
NQ = P // Q
ROWS = 512
G = ROWS // Q
EPS = 1e-5

SECTION = 26
PIECE = 9
PART = 3
RAWS = 3
SPLITS = 3
TURNS = 6
ON_VECTOR = (3, 9, 15)
EARLY = (19, 21, 23)
LAG = 2


def column_plan(n):
    stride = SECTION * Q
    sections = n // (NQ * stride)
    last = n - (NQ - 1) * stride - (SECTION + 1) * Q
    plan = [(s * NQ * stride, SECTION) for s in range(sections - 1)] + [(last, SECTION + 1)]
    return stride, plan, (sections - 1) * NQ * stride - last


def gnn_layer(nc, x, adj, item_feat, w_item, b_item, w_user, b_user, out):
    N = adj.shape[0]
    stride, plan, seam = column_plan(N)
    PIECES = [(s, b0, min(PIECE, blocks - b0)) for s, (_, blocks) in enumerate(plan) for b0 in range(0, blocks, PIECE)]
    NPC = len(PIECES)
    PARTS = []
    for k, (_, _, nb) in enumerate(PIECES):
        PARTS += [(k, True, 0, PART), (k, True, nb - PART, nb), (k, False, PART, nb - PART)]
    NP = len(PARTS)
    SPLIT = [p for p in range(NP) if PARTS[p][1]]
    WHOLE = [p for p in range(NP) if not PARTS[p][1]]
    NS, NW = len(SPLIT), len(WHOLE)
    LOW_AFTER = {SPLIT[s + LAG]: s for s in ON_VECTOR}
    ON_DVE = sorted(LOW_AFTER.values())
    ON_POOL = [s for s in range(NS) if s not in ON_DVE]
    FULL = N // ROWS
    TAIL = -(-(N - FULL * ROWS) // Q) * Q
    NB = FULL + 1
    PAIRS = NB // 2
    assert PIECES[-1][2] == PIECE and all(nb < PIECE for _, _, nb in PIECES[(NPC - 1) % RAWS:-1:RAWS])
    assert NB % 2 == 0 and NPC % RAWS == 0 and NS % SPLITS == 0 and 2 * NP % TURNS == 0

    def tiles(rows):
        return [(t, min(P, rows - t * P)) for t in range(-(-rows // P))]

    def runs(rows):
        full = rows // P
        return [(P, 0, full)] + ([(rows - full * P, full, full + 1)] if rows % P else [])

    ctx = ExitStack()
    with ctx:
        def sb(name, shape, dt=FP32):
            return ctx.enter_context(nc.sbuf_tensor(name, shape, dt))

        def pb(name):
            return ctx.enter_context(nc.psum_tensor(name, [P, ROWS], FP32))

        def sem(name):
            return ctx.enter_context(nc.semaphore(name))

        raw = [sb(f"raw{s}", [P, G, PIECE * Q]) for s in range(RAWS)]
        adjT = sb("adjT", [P, TURNS, G, PART * Q])
        high = [sb(f"high{s}", [P, G, PART * Q], FP32R) for s in range(SPLITS)]
        low = [sb(f"low{s}", [P, G, PART * Q], FP32R) for s in range(SPLITS)]
        h_high = sb("h_high", [P, NS, PART, P], FP32R)
        h_low = sb("h_low", [P, NS, PART, P], FP32R)
        h_full = sb("h_full", [P, NW, PART, P])
        ident = sb("ident", [P, P])
        wT = sb("wT", [P, 2, P])
        b_item_all = sb("b_item_all", [P, P])
        b_user_col = sb("b_user_col", [P, 1])
        x_nat = [sb(f"x_nat{s}", [P, 4, P]) for s in range(2)]
        xT = sb("xT", [P, ROWS])
        actT = sb("actT", [P, ROWS])
        y = [sb(f"y{s}", [P, 4, P]) for s in range(2)]
        stats = sb("stats", [P, 4, 6])
        mv = sb("mv", [P, 4, 2])
        std = sb("std", [P, 4])
        rstd = sb("rstd", [P, 4])
        eps = sb("eps", [P, 1])
        gate = sb("gate", [P, 1])

        acc = [pb(f"acc{s}") for s in range(2)]
        four_banks = ctx.enter_context(nc.psum_tensor("four_banks", [P, 4 * ROWS], FP32))
        featT_ps = [four_banks[:, s * ROWS:(s + 1) * ROWS] for s in (0, 1)]
        h_ps = [four_banks[:, s * ROWS:(s + 1) * ROWS] for s in (2, 3)]
        high_ps = four_banks[:, 0:G * PART * Q].rearrange("p (g w) -> p g w", g=G)
        xT_ps = pb("xT_ps")
        y_ps = pb("y_ps")

        w_nat = x_nat[1][:, 0:2, :]
        featT = [t[:, 0:PART * P].rearrange("p (b f) -> p b f", f=P) for t in (xT, actT)]
        h_stage = [t[:, 0:PART, :] for t in y]
        feat_at = [v.rearrange("p (b f) -> p b f", f=P)[:, 0:blocks, :] for (_, blocks), v in zip(
            plan, [adjT[:, :, :, :].rearrange("p a g w -> p (a g w)")]
            + [raw[s][:, :, :].rearrange("p g w -> p (g w)") for s in (1, 2)])]

        w_loaded = sem("w_loaded")
        b_loaded = sem("b_loaded")
        feat_loaded = [sem(f"feat_loaded{s}") for s in range(NPC)]
        x_loaded = [sem(f"x_loaded{s}") for s in range(2)]
        raw_loaded = [sem(f"raw_loaded{s}") for s in range(RAWS)]
        ident_step = sem("ident_step")
        wT_done = sem("wT_done")
        wT_copied = sem("wT_copied")
        featT_done = sem("featT_done")
        featT_copied = sem("featT_copied")
        h_done = sem("h_done")
        h_biased = sem("h_biased")
        h_masked = sem("h_masked")
        h_high_done = sem("h_high_done")
        h_low_done = sem("h_low_done")
        turned = sem("turned")
        high_done = sem("high_done")
        high_ps_done = sem("high_ps_done")
        low_by_pool = sem("low_by_pool")
        low_by_dve = sem("low_by_dve")
        split_used = sem("split_used")
        whole_used = sem("whole_used")
        xT_done = sem("xT_done")
        xT_copied = sem("xT_copied")
        xT_used = sem("xT_used")
        relu_done = sem("relu_done")
        y_turned = sem("y_turned")
        y_added = sem("y_added")
        stats_done = sem("stats_done")
        mv_done = sem("mv_done")
        std_done = sem("std_done")
        rstd_done = sem("rstd_done")
        normed = sem("normed")
        stored = [sem(f"stored{s}") for s in range(2)]
        eps_set = sem("eps_set")
        pad_zeroed = sem("pad_zeroed")
        block = ctx.enter_context(nc.Block())

        GROUPS = [(k, split, PIECES[k][1] + lo, hi - lo) for k, split, lo, hi in PARTS]
        READ = [sum(3 for s, _, _ in PIECES if s <= t) for t in range(len(plan))]
        MASKED = [g for g, (k, _, b, m) in enumerate(GROUPS) if PIECES[k][0] == len(plan) - 1 and (b == 0 or b + m == plan[-1][1])]

        def wait(eng, semaphore, count):
            if not (isinstance(count, int) and count <= 0):
                eng.wait_ge(semaphore, count)

        def over_blocks(eng, body):
            body(0, ROWS, 0, 0)
            body(ROWS, ROWS, 1, 1)
            with eng.Fori(1, PAIRS - 1) as i:
                body(i * (2 * ROWS), ROWS, i * 2, 0)
                body(i * (2 * ROWS) + ROWS, ROWS, i * 2 + 1, 1)
            body((NB - 2) * ROWS, ROWS, NB - 2, 0)
            body(N - TAIL, TAIL, NB - 1, 1)

        def is_first(n):
            return isinstance(n, int) and n == 0

        def x_total(n, rows, par):
            return (n - par) * (8 * len(runs(ROWS))) + 16 * len(runs(rows))

        def t_slot(p, par):
            return (NP * par + p) % TURNS

        def load_feat(eng, k, quarters):
            s, b0, nb = PIECES[k]
            for q in quarters:
                row = plan[s][0] + stride * q + Q * b0
                eng.dma_start(feat_at[s][Q * q:Q * (q + 1), b0:b0 + nb, :],
                              item_feat[row:row + Q * nb, :].rearrange("(b j) f -> j b f", j=Q)).then_inc(feat_loaded[k], 16)

        def load_piece(eng, k, row, rows, quarters):
            s, b0, nb = PIECES[k]
            for q in quarters:
                col = plan[s][0] + stride * q + Q * b0
                w = nb * Q if k < NPC - 1 or q == NQ - 1 else (nb - 1) * Q
                eng.dma_start(raw[k % RAWS][Q * q:Q * (q + 1), 0:rows // Q, 0:w],
                              adj[bass.ds(row, rows), col:col + w].rearrange("(g i) c -> i g c", i=Q)
                              ).then_inc(raw_loaded[k % RAWS], 16)

        @block.sync
        def _(sp):
            for k in range(NPC):
                load_feat(sp, k, (0, 2, 1, 3))

            def load_block(row, rows, n, par):
                if isinstance(n, int) and n == 1:
                    sp.wait_ge(wT_done, 1)
                wait(sp, y_added, n - 1)
                for m, lo, hi in runs(rows):
                    sp.dma_start(x_nat[par][0:m, lo:hi, :],
                                 x[bass.ds(row + lo * P, (hi - lo) * m), :].rearrange("(t p) f -> p t f", p=m)
                                 ).then_inc(x_loaded[par], 16)
                for k in range(NPC):
                    wait(sp, turned, (n * NPC + (k - RAWS + 1)) * 3)
                    if is_first(n) and k in (1, 2):
                        sp.wait_ge(featT_done, READ[k])
                    load_piece(sp, k, row, rows, (0, 1))

            over_blocks(sp, load_block)

        @block.gpsimd
        def _(pool):
            nc.gpsimd.memset(ident[:, :], 0.0).then_inc(ident_step, 1)
            pool.wait_ge(ident_step, 1)
            nc.gpsimd.affine_select(out=ident[:, :], in_=ident[:, :], compare_op=ALU.not_equal, fill=1.0,
                                    base=0, pattern=[[-1, P]], channel_multiplier=1).then_inc(ident_step, 1)
            for i in range(NS):
                pool.wait_ge(h_high_done, i + 1)
                nc.gpsimd.tensor_tensor(h_low[:, i, :, :], h_stage[i % 2], h_high[:, i, :, :].bitcast(FP32),
                                        ALU.subtract).then_inc(h_low_done, 1)

            pool.wait_ge(featT_done, len(GROUPS))
            nc.gpsimd.memset(raw[(NPC - 1) % RAWS][0:(NQ - 1) * Q, :, (PIECE - 1) * Q:PIECE * Q], 0.0).then_inc(pad_zeroed, 1)

            def low_parts(row, rows, n, par):
                for i, s in enumerate(ON_POOL):
                    pool.wait_ge(high_done, n * NS + s + 1)
                    wait(pool, split_used, n * NS + s + 1 - SPLITS)
                    nc.gpsimd.tensor_tensor(low[s % SPLITS][:, 0:rows // Q, :], adjT[:, t_slot(SPLIT[s], par), 0:rows // Q, :],
                                            high[s % SPLITS][:, 0:rows // Q, :].bitcast(FP32), ALU.subtract
                                            ).then_inc(low_by_pool, 1)

            over_blocks(pool, low_parts)

        def wait_low(eng, n, s):
            if s in ON_DVE:
                wait(eng, low_by_dve, n * len(ON_DVE) + ON_DVE.index(s) + 1)
            else:
                wait(eng, low_by_pool, n * len(ON_POOL) + ON_POOL.index(s) + 1)

        @block.tensor
        def _(pe):
            pe.wait_ge(ident_step, 2)
            pe.wait_ge(w_loaded, 32)
            for w in range(2):
                last = nc.tensor.transpose(xT_ps[:, w * P:(w + 1) * P], w_nat[:, w, :], ident[:, :])
            last.then_inc(wT_done, 1)

            def turn_feat(g):
                k, _, b, m = GROUPS[g]
                s = PIECES[k][0]
                wait(pe, featT_copied, g - 1)
                pe.wait_ge(feat_loaded[k], 16 * NQ)
                for r in range(m):
                    last = nc.tensor.transpose(featT_ps[g % 2][:, r * P:(r + 1) * P], feat_at[s][:, b + r, :], ident[:, :])
                last.then_inc(featT_done, 1)

            def make_h(g):
                m = GROUPS[g][3]
                pe.wait_ge(featT_copied, g + 1)
                wait(pe, h_biased, g - 1)
                for r in range(m):
                    last = nc.tensor.matmul(h_ps[g % 2][:, r * P:(r + 1) * P], featT[g % 2][:, r, :], wT[:, 0, :],
                                            start=True, stop=True)
                last.then_inc(h_done, 1)

            turn_feat(0)
            pe.wait_ge(wT_copied, 1)
            for g in range(len(GROUPS)):
                if g + 1 < len(GROUPS):
                    turn_feat(g + 1)
                make_h(g)

            def turn_x(n, rows, par):
                pe.wait_ge(x_loaded[par], x_total(n, rows, par))
                wait(pe, xT_copied, n)
                for t, m in tiles(rows):
                    last = nc.tensor.transpose(xT_ps[:, t * P:t * P + m], x_nat[par][0:m, t, :], ident[0:m, 0:m])
                last.then_inc(xT_done, 1)

            def turn_back(n, rows):
                pe.wait_ge(relu_done, n + 1)
                wait(pe, normed, n)
                for t, m in tiles(rows):
                    last = nc.tensor.transpose(y_ps[0:m, t * P:(t + 1) * P], actT[:, t * P:t * P + m], ident[:, :])
                last.then_inc(y_turned, 1)

            def product(row, rows, n, par):
                g = rows // Q
                total = acc[par][:, 0:rows].rearrange("p (g i) -> p g i", i=Q)

                def add(weights, moving, b, first=False, final=False):
                    return nc.tensor.matmul(total, weights, moving[:, 0:g, b * Q:(b + 1) * Q], start=first, stop=final)

                wait(pe, relu_done, n - 1)
                for k in range(NPC):
                    if is_first(n):
                        pe.wait_ge(h_biased, 3 * (k + 1))
                        ready = sum(p < 3 * (k + 1) for p in SPLIT)
                        pe.wait_ge(h_high_done, ready)
                        pe.wait_ge(h_low_done, ready)
                    mine = [p for p in range(NP) if PARTS[p][0] == k]
                    for p in sorted(mine, key=lambda p: PARTS[p][1]):
                        _, split, b_lo, b_hi = PARTS[p]
                        if not split:
                            i = WHOLE.index(p)
                            pe.wait_ge(turned, n * NP + p + 1)
                            for b in range(b_hi - b_lo):
                                last = add(h_full[:, i, b, :], adjT[:, t_slot(p, par), :, :], b, first=(k == 0 and b == 0))
                            last.then_inc(whole_used, 1)
                            continue
                        s = SPLIT.index(p)
                        hi, lo = high[s % SPLITS], low[s % SPLITS]
                        pe.wait_ge(high_done, n * NS + s + 1)
                        for b in range(PART):
                            add(h_high[:, s, b, :], hi, b)
                            add(h_low[:, s, b, :], hi, b)
                        wait_low(pe, n, s)
                        for b in range(PART):
                            last = add(h_high[:, s, b, :], lo, b, final=(s == NS - 1 and b == PART - 1))
                        last.then_inc(split_used, 1)
                    if k == 0 and not is_first(n):
                        turn_back(n - 1, ROWS)
                    if k == 1:
                        turn_x(n, rows, par)
                    if k == 3:
                        pe.wait_ge(xT_copied, n + 1)
                        nc.tensor.matmul(acc[par][:, 0:rows], wT[:, 1, :], xT[:, 0:rows], start=False, stop=False
                                         ).then_inc(xT_used, 1)

            over_blocks(pe, product)
            turn_back(NB - 1, TAIL)

        @block.scalar
        def _(act):
            act.dma_start(w_nat[:, 0, :], w_item).then_inc(w_loaded, 16)
            act.dma_start(w_nat[:, 1, :], w_user).then_inc(w_loaded, 16)
            act.dma_start(b_item_all[:, :], b_item.rearrange("(a n) -> a n", a=1).to_broadcast([P, P])
                         ).then_inc(b_loaded, 16)
            act.dma_start(b_user_col[:, :], b_user.rearrange("(n a) -> n a", a=1)).then_inc(b_loaded, 16)
            act.wait_ge(wT_done, 1)
            nc.scalar.activation(wT[:, :, :].rearrange("p w h -> p (w h)"), xT_ps[:, 0:2 * P], ACT.Copy
                                 ).then_inc(wT_copied, 1)

            def copy_featT(g):
                m = GROUPS[g][3]
                act.wait_ge(featT_done, g + 1)
                wait(act, h_done, g - 1)
                nc.scalar.activation(featT[g % 2][:, 0:m, :].rearrange("p b f -> p (b f)"), featT_ps[g % 2][:, 0:m * P],
                                     ACT.Copy).then_inc(featT_copied, 1)

            def split_h(i):
                g = SPLIT[i]
                act.wait_ge(h_biased, g + 1)
                if g in MASKED:
                    act.wait_ge(h_masked, MASKED.index(g) + 1)
                nc.scalar.activation(h_high[:, i, :, :], h_stage[i % 2], ACT.Copy).then_inc(h_high_done, 1)

            for g in range(len(GROUPS)):
                copy_featT(g)
                if g == 2:
                    load_piece(act, 0, 0, ROWS, (2, 3))
                for k in (1, 2):
                    if g == READ[k]:
                        load_piece(act, k, 0, ROWS, (2, 3))
                if g >= 2 and g - 2 in SPLIT:
                    split_h(SPLIT.index(g - 2))
            for g in SPLIT:
                if g + 2 >= len(GROUPS):
                    split_h(SPLIT.index(g))

            if READ[2] == len(GROUPS):
                load_piece(act, 2, 0, ROWS, (2, 3))
            act.wait_ge(eps_set, 1)
            act.wait_ge(b_loaded, 32)

            def deviation(n, rows):
                act.wait_ge(mv_done, n + 1)
                wait(act, rstd_done, n)
                w = len(tiles(rows))
                nc.scalar.activation(std[:, 0:w], mv[:, 0:w, 1], ACT.Sqrt, bias=eps[:, 0:1]).then_inc(std_done, 1)

            def store(n, row, rows, par):
                act.wait_ge(normed, n + 1)
                for m, lo, hi in runs(rows):
                    act.dma_start(out[bass.ds(row + lo * P, (hi - lo) * m), :].rearrange("(t p) f -> p t f", p=m),
                                  y[par][0:m, lo:hi, :]).then_inc(stored[par], 16)

            def store_last(n, row, rows, par, skip):
                act.wait_ge(normed, n + 1)
                for t, m in tiles(rows):
                    s = skip if t == 0 else 0
                    act.dma_start(out[row + t * P + s:row + t * P + m, :], y[par][s:m, t, :]).then_inc(stored[par], 16)

            def relu(n, rows, par):
                act.wait_ge(split_used, (n + 1) * NS)
                wait(act, y_turned, n)
                nc.scalar.activation(actT[:, 0:rows], acc[par][:, 0:rows], ACT.Relu,
                                     bias=b_user_col[:, 0:1]).then_inc(relu_done, 1)

            def high_parts(row, rows, n, par):
                before = row - ROWS if rows == ROWS else (NB - 2) * ROWS
                for s in range(NS):
                    k = PARTS[SPLIT[s]][0]
                    act.wait_ge(turned, n * NP + SPLIT[s] + 1)
                    wait(act, split_used, n * NS + s + 1 - SPLITS)
                    nc.scalar.activation(high[s % SPLITS][:, 0:rows // Q, :], adjT[:, t_slot(SPLIT[s], par), 0:rows // Q, :],
                                         ACT.Copy).then_inc(high_done, 1)
                    if s in ON_DVE:
                        if is_first(n) and s == ON_DVE[0]:
                            act.wait_ge(h_biased, NP)
                        wait(act, low_by_dve, n * len(ON_DVE) + ON_DVE.index(s))
                        nc.scalar.activation(high_ps[:, 0:rows // Q, :].bitcast(FP32R), adjT[:, t_slot(SPLIT[s], par), 0:rows // Q, :],
                                             ACT.Copy).then_inc(high_ps_done, 1)
                    if s < NS - 1 and PARTS[SPLIT[s + 1]][0] == k:
                        continue
                    if k < NPC - RAWS:
                        act.wait_ge(turned, (n * NPC + k + 1) * 3)
                        load_piece(act, k + RAWS, row, rows, (2, 3))
                    elif rows == ROWS:
                        act.wait_ge(turned, (n * NPC + k + 1) * 3)
                        nxt = (N - TAIL, TAIL) if isinstance(n, int) and n == NB - 2 else (row + ROWS, ROWS)
                        load_piece(act, k + RAWS - NPC, *nxt, (2, 3))
                    if k == 0 and not is_first(n):
                        relu(n - 1, ROWS, 1 - par)
                    if k == 2:
                        act.wait_ge(xT_done, n + 1)
                        wait(act, xT_used, n)
                        nc.scalar.activation(xT[:, 0:rows], xT_ps[:, 0:rows], ACT.Copy).then_inc(xT_copied, 1)
                    if k == 4 and not is_first(n):
                        deviation(n - 1, ROWS)
                    if k == 6 and not is_first(n):
                        store(n - 1, before, ROWS, 1 - par)

            over_blocks(act, high_parts)
            relu(NB - 1, TAIL, 1)
            deviation(NB - 1, TAIL)
            store_last(NB - 1, N - TAIL, TAIL, 1, FULL * ROWS - (N - TAIL))
            for par in range(2):
                act.wait_ge(stored[par], 16 * sum(len(tiles(TAIL)) if n == NB - 1 else len(runs(ROWS)) for n in range(par, NB, 2)))

        @block.vector
        def _(dve):
            nc.vector.memset(eps[:, :], EPS).then_inc(eps_set, 1)
            dve.wait_ge(b_loaded, 32)

            def bias_h(g):
                k, split, b, m = GROUPS[g]
                dve.wait_ge(h_done, g + 1)
                if split:
                    i = SPLIT.index(g)
                    wait(dve, h_low_done, i - 1)
                    dst = h_stage[i % 2]
                else:
                    dst = h_full[:, WHOLE.index(g), 0:m, :]
                last = nc.vector.tensor_tensor(dst, h_ps[g % 2][:, 0:m * P].rearrange("p (b f) -> p b f", f=P),
                                               b_item_all[:, :].unsqueeze(1).to_broadcast([P, m, P]), ALU.add)
                last.then_inc(h_biased, 1)
                if g in MASKED:
                    dve.wait_ge(h_biased, g + 1)
                    if g == MASKED[0]:
                        nc.vector.memset(h_stage[i % 2][0:seam, 0, :], 0.0).then_inc(h_masked, 1)
                    else:
                        nc.vector.memset(h_stage[i % 2][0:(NQ - 1) * Q, m - 1, :], 0.0).then_inc(h_masked, 1)

            def turn(k, rows, n, par):
                for p in range(3 * k, 3 * k + 3):
                    turn_part(p, rows, n, par)

            def turn_part(p, rows, n, par):
                k, _, lo, hi = PARTS[p]
                if is_first(n) and k == NPC - 1:
                    dve.wait_ge(pad_zeroed, 1)
                dve.wait_ge(raw_loaded[k % RAWS], (n * (NPC // RAWS) + (k // RAWS + 1)) * (16 * NQ))
                before, nb = (p - TURNS, n) if p >= TURNS else (p - TURNS + NP, None if is_first(n) else n - 1)
                if nb is not None and PARTS[before][1]:
                    wait_low(dve, nb, SPLIT.index(before))
                elif nb is not None:
                    dve.wait_ge(whole_used, nb * NW + WHOLE.index(before) + 1)
                nc.vector.transpose(adjT[:, t_slot(p, par), 0:rows // Q, 0:(hi - lo) * Q],
                                    raw[k % RAWS][:, 0:rows // Q, lo * Q:hi * Q]).then_inc(turned, 1)
                if p in LOW_AFTER:
                    low_part(LOW_AFTER[p], rows, n, par)

            def low_part(s, rows, n, par):
                dve.wait_ge(high_ps_done, n * len(ON_DVE) + ON_DVE.index(s) + 1)
                wait(dve, split_used, n * NS + s + 1 - SPLITS)
                nc.vector.tensor_tensor(low[s % SPLITS][:, 0:rows // Q, :], adjT[:, t_slot(SPLIT[s], par), 0:rows // Q, :],
                                        high_ps[:, 0:rows // Q, :], ALU.subtract
                                        ).then_inc(low_by_dve, 1)

            def add_and_stats(n, rows, par):
                dve.wait_ge(y_turned, n + 1)
                dve.wait_ge(x_loaded[par], x_total(n, rows, par))
                for m, lo, hi in runs(rows):
                    at = y_ps[0:m, lo * P:hi * P].rearrange("p (t f) -> p t f", f=P)
                    last = nc.vector.tensor_tensor(at, at, x_nat[par][0:m, lo:hi, :], ALU.add)
                last.then_inc(y_added, 1)
                dve.wait_ge(y_added, n + 1)
                for t, m in tiles(rows):
                    last = nc.vector.bn_stats(stats[0:m, t, :], y_ps[0:m, t * P:(t + 1) * P])
                last.then_inc(stats_done, 1)
                dve.wait_ge(stats_done, n + 1)
                wait(dve, std_done, n)
                nc.vector.memset(gate[:, :], 0.0)
                for t, m in tiles(rows):
                    last = nc.vector.bn_aggr(mv[0:m, t, :], stats[0:m, t, :])
                last.then_inc(mv_done, 1)

            def normalise(n, rows, par):
                w = len(tiles(rows))
                dve.wait_ge(std_done, n + 1)
                nc.vector.reciprocal(rstd[:, 0:w], std[:, 0:w]).then_inc(rstd_done, 1)
                dve.wait_ge(rstd_done, n + 1)
                wait(dve, stored[par], (n - par) * (8 * len(runs(ROWS))))
                for t, m in tiles(rows):
                    last = nc.vector.tensor_scalar(y[par][0:m, t, :], y_ps[0:m, t * P:(t + 1) * P], mv[0:m, t, 0:1], rstd[0:m, t:t + 1],
                                                   ALU.subtract, ALU.mult)
                last.then_inc(normed, 1)

            def transposes(row, rows, n, par):
                for k in range(NPC):
                    if not (is_first(n) and k == 0):
                        turn(k, rows, n, par)
                    if k == 2 and not is_first(n):
                        add_and_stats(n - 1, ROWS, 1 - par)
                    if k == 5 and not is_first(n):
                        normalise(n - 1, ROWS, 1 - par)

            for g in range(len(GROUPS)):
                bias_h(g)
                if g in EARLY:
                    turn_part(EARLY.index(g), ROWS, 0, 0)
            over_blocks(dve, transposes)
            add_and_stats(NB - 1, TAIL, 1)
            normalise(NB - 1, TAIL, 1)


_INS = ["x", "adj", "L0_gnn_item_feat", "L0_gnn_W_item", "L0_gnn_b_item", "L0_gnn_W_user", "L0_gnn_b_user"]


def kernel(**inputs):
    import numpy as _np
    import concourse.bacc as _bacc
    from concourse import mybir as _mybir
    from concourse.bass_utils import run_bass_kernel_spmd as _run

    nc = _bacc.Bacc("TRN2", target_bir_lowering=False, num_devices=1, dynamic_dma_scratch_size=1024)
    arrays, args = {}, []
    for name in _INS:
        a = _np.ascontiguousarray(inputs[name])
        arrays[f"in_{name}_dram"] = a
        args.append(nc.dram_tensor(f"in_{name}_dram", a.shape, _mybir.dt.from_np(a.dtype), kind="ExternalInput").ap())
    out = nc.dram_tensor("out_dram", inputs["x"].shape, _mybir.dt.float32, kind="ExternalOutput").ap()
    gnn_layer(nc, *args, out)
    r = _run(nc, [arrays], core_ids=[0])
    return r.results[0]["out_dram"]
```
